# Optimizing a Trainium2 kernel written in Bass

```python
import numpy as np
import jax
import jax.numpy as jnp

def _softmax(x, axis=-1):
    return jax.nn.softmax(x, axis=axis)
def _gelu(x):
    return jax.nn.gelu(x, approximate=True)
def _silu(x):
    return jax.nn.silu(x)
def _sigmoid(x):
    return jax.nn.sigmoid(x)
def _layernorm(x, axis=-1, eps=1e-5):
    m = jnp.mean(x, axis=axis, keepdims=True)
    v = jnp.var(x, axis=axis, keepdims=True)
    return (x - m) / jnp.sqrt(v + eps)
def _scatter_add(tgt, idx, src, axis=0):
    return tgt.at[idx].add(src)
def _segment_sum(src, seg, n):
    return jax.ops.segment_sum(src, seg, n)

kernel_name = 'mk_conv_preact_d1_conv_nhwc256_6165e3'

def setup_inputs(seed: int = 0):
    np.random.seed(seed)
    _w = jnp.asarray
    def _rec_inputs():
        import jax
        import jax.numpy as jnp
        _gk = jax.random.key(seed)
        x = 1.508e-05 + 1 * jax.random.normal(jax.random.fold_in(_gk, 1), (4, 256, 256, 256), jnp.float32)
        return x
    x = _rec_inputs()
    def _L0_conv_setup():
        import jax, jax.numpy as jnp
        import numpy as np
        DB4 = np.array([0.23037781330885523, 0.7148465705525415, 0.6308807679295904, -0.02798376941698385, -0.18703481171888114, 0.030841381835986965, 0.032883011666982945, -0.010597401784997278], dtype=np.float32)

        def _corr_valid(u, f):
            L = f.shape[0]
            B = int(np.prod(u.shape[:-1]))
            out = jax.lax.conv_general_dilated(u.reshape(B, 1, u.shape[-1]), f.reshape(1, 1, L), window_strides=(1,), padding='VALID', dimension_numbers=('NCW', 'OIW', 'NCW'))
            return out.reshape(u.shape[:-1] + (out.shape[-1],))

        def _recon_axis(s, w, h0, h1, axis):
            L = h0.shape[0]
            P = (L - 2) // 2 + 1
            x = jnp.stack([s, w])
            x = jnp.moveaxis(x, axis + 1, -1)
            N = x.shape[-1]
            x = jnp.concatenate([x[..., N - P:], x], axis=-1)[..., 1:]
            up = jnp.stack([jnp.zeros_like(x), x], axis=-1).reshape(x.shape[:-1] + (-1,))
            up = jnp.pad(up, [(0, 0)] * (up.ndim - 1) + [(0, 1)])
            y = _corr_valid(up[0], h0) + _corr_valid(up[1], h1)
            return jnp.moveaxis(y, -1, axis)
        key = jax.random.key(seed)
        x = jax.random.normal(key, (4, 256, 256, 256), dtype=jnp.float32)
        h = jnp.asarray(DB4)
        return {'x': x, 'h': h}
    _L0_conv_all = _L0_conv_setup()
    _L0_conv_in = {k: v for k, v in _L0_conv_all.items() if k in ('h', )}
    del _L0_conv_all

    return {
        "x": x,
        "L0_conv_h": _L0_conv_in["h"],
    }

def reference(x, L0_conv_h):
    import jax
    import jax.numpy as jnp
    def _L0_conv_ref(x, h):
        import jax, jax.numpy as jnp
        import numpy as np
        DB4 = np.array([0.23037781330885523, 0.7148465705525415, 0.6308807679295904, -0.02798376941698385, -0.18703481171888114, 0.030841381835986965, 0.032883011666982945, -0.010597401784997278], dtype=np.float32)

        def _corr_valid(u, f):
            L = f.shape[0]
            B = int(np.prod(u.shape[:-1]))
            out = jax.lax.conv_general_dilated(u.reshape(B, 1, u.shape[-1]), f.reshape(1, 1, L), window_strides=(1,), padding='VALID', dimension_numbers=('NCW', 'OIW', 'NCW'))
            return out.reshape(u.shape[:-1] + (out.shape[-1],))

        def _recon_axis(s, w, h0, h1, axis):
            L = h0.shape[0]
            P = (L - 2) // 2 + 1
            x = jnp.stack([s, w])
            x = jnp.moveaxis(x, axis + 1, -1)
            N = x.shape[-1]
            x = jnp.concatenate([x[..., N - P:], x], axis=-1)[..., 1:]
            up = jnp.stack([jnp.zeros_like(x), x], axis=-1).reshape(x.shape[:-1] + (-1,))
            up = jnp.pad(up, [(0, 0)] * (up.ndim - 1) + [(0, 1)])
            y = _corr_valid(up[0], h0) + _corr_valid(up[1], h1)
            return jnp.moveaxis(y, -1, axis)
        h0 = h[::-1]
        sign = jnp.where(jnp.arange(h.shape[0]) % 2 == 0, -1.0, 1.0).astype(h.dtype)
        h1 = sign * h
        out = x
        for axis in range(1, x.ndim):
            s, w = jnp.split(out, 2, axis=axis)
            out = _recon_axis(s, w, h0, h1, axis)
        return out

    def _gn(v, G=32, eps=1e-5):
        B_, H_, W_, C_ = v.shape
        g = v.reshape(B_, H_, W_, G, C_ // G)
        m = jnp.mean(g, axis=(1, 2, 4), keepdims=True)
        s = jnp.var(g, axis=(1, 2, 4), keepdims=True)
        return ((g - m) / jnp.sqrt(s + eps)).reshape(v.shape)

    def _ln_c(v, eps=1e-6):
        m = jnp.mean(v, axis=-1, keepdims=True)
        s = jnp.var(v, axis=-1, keepdims=True)
        return (v - m) / jnp.sqrt(s + eps)

    def _ln_t(v, eps=1e-5):
        m = jnp.mean(v, axis=-1, keepdims=True)
        s = jnp.var(v, axis=-1, keepdims=True)
        return (v - m) / jnp.sqrt(s + eps)

    def _to_tokens(v):
        B_, H_, W_, C_ = v.shape
        return v.reshape(B_, H_ * W_, C_)
    def _from_tokens(t, like):
        return t.reshape(like.shape)

    x = x + _L0_conv_ref(_gn(x), L0_conv_h)
    return x


_drawn_inputs = setup_inputs


def setup_inputs(seed=0):
    import zlib

    import numpy as np

    out = dict(_drawn_inputs(seed))
    spreads = {}
    factors = {}
    for name, (base, spread) in spreads.items():
        noise = np.random.default_rng([zlib.crc32(name.encode()), seed]).standard_normal(out[name].shape)
        drawn = base * np.exp(spread * noise) if base else spread * noise
        out[name] = jnp.asarray(drawn.astype(out[name].dtype))
    for name, factor in factors.items():
        out[name] = (out[name] * factor).astype(out[name].dtype)
    return out
```

```python
from contextlib import ExitStack

import numpy as np

import concourse.bass as bass
from concourse import mybir

P = 128
B, H, W, C = 4, 256, 256, 256
PAIRS = 128
TAPS = 8
GROUPS = 32
GC = C // GROUPS
EPS = 1e-5

CP = 4
CHUNKS = PAIRS // CP
ROWS = 2 * CP
WP = 4
TILES = PAIRS // WP
UNITS = 4
TPU = TILES // UNITS
UW = W // UNITS
HALO = TAPS - 2
N1 = (2 * WP + HALO) * ROWS
NC2 = P + HALO
RING = 8
QS = 4
POS = 16
ST_TILES = H * W // (P * POS)
UPB = CHUNKS * UNITS
assert ST_TILES == CHUNKS and 2 * UNITS == RING

O_H, O_W = 0, 2 * ROWS
O_C = O_W + 2 * WP + HALO
O_S = O_C + NC2
NCOEF = O_S + 2

F32 = mybir.dt.float32
ALU = mybir.AluOpType
ACT = mybir.ActivationFunctionType
AX = mybir.AxisListType


def tap_table():
    t = np.zeros((P, TAPS, NCOEF), np.float32)

    def put(p, col, high, d):
        if 0 <= d < TAPS:
            if high:
                t[p, TAPS - 1 - d, col] = 1.0 if d % 2 == 0 else -1.0
            else:
                t[p, d, col] = 1.0

    for p in range(P):
        strip, rest = p % 2, p // 2
        hh, hi, wh, wi = rest // 32, rest // 8 % 4, rest // 4 % 2, rest % 4
        for phase in range(2):
            for n in range(ROWS):
                put(p, O_H + phase * ROWS + n, hh, n - 2 * hi + (0 if strip == phase else ROWS))
        for n in range(2 * WP + HALO):
            put(p, O_W + n, wh, n - 2 * wi)
        for n in range(NC2):
            put(p, O_C + n, p // 64, n - 2 * (p % 64))
    for i in range(TAPS):
        t[:, i, O_S] = 1.0
        t[:, i, O_S + 1] = 1.0 if i % 2 else -1.0
    return t


def group_masks():
    m = np.zeros((P, 2, GROUPS), np.float32)
    for ct in range(2):
        for p in range(P):
            c = (0 if p < 64 else 128) + 64 * ct + p % 64
            m[p, ct, c // GC] = 1.0
    return m


def wavelet_preact_kernel(nc, x, h, taps, gmask, out):
    x_rows = x.rearrange("b h w c -> (b h) (w c)")
    out_rows = out.rearrange("b h w c -> (b h) (w c)")
    x_strip = x.rearrange("b h (v t i) c -> i (b h v) t c", v=2, i=WP)
    x_strip_t = x.rearrange("b h (v t i) c -> t (b h v) i c", v=2, i=WP)
    x_stats = x.rearrange("b h w c -> (b h w c)").rearrange("(n p f) -> n p f", p=P, f=POS * C)

    with ExitStack() as ctx:
        def sb(name, shape):
            return ctx.enter_context(nc.sbuf_tensor(name, shape, F32))

        def sem(name):
            return ctx.enter_context(nc.semaphore(name))

        strip = sb("strip", [P, TILES, C])
        stats_in = [sb(f"stats_in{s}", [P, POS * C]) for s in range(2)]
        resid = [sb(f"resid{s}", [P, QS * C]) for s in range(RING)]
        y1 = [[sb(f"y1_{s}{ct}", [P, UW * ROWS]) for ct in range(2)] for s in range(2)]
        records = sb("records", [P, ST_TILES, GROUPS, 6])
        dev = sb("dev", [P, ST_TILES, GROUPS, 2])
        dev2 = sb("dev2", [P, ST_TILES, GROUPS, 2])
        taps_sb = sb("taps_sb", [P, TAPS, NCOEF])
        mask_sb = sb("mask_sb", [P, 2, GROUPS])
        h_sb = sb("h_sb", [P, TAPS])
        coef = [sb(f"coef{s}", [P, NCOEF]) for s in range(2)]
        m_hw = sb("m_hw", [P, 2, N1])
        ones = sb("ones", [P, P])
        part = sb("part", [P, GROUPS])
        gstat = sb("gstat", [P, 2, GROUPS])
        var_sb = sb("var_sb", [P, GROUPS])
        std_sb = sb("std_sb", [P, GROUPS])
        junk = sb("junk", [P, GROUPS])
        chan = sb("chan", [P, 2, 2])
        neg_mr = sb("neg_mr", [P, 2])
        row_sums = sb("row_sums", [P, 2, P])
        mean_lhs = sb("mean_lhs", [P, 2, 2, P])
        m_cr = sb("m_cr", [P, 2, NC2])
        means_w3 = sb("means_w3", [P, 2 * C])

        ps1 = [[ctx.enter_context(nc.psum_tensor(f"ps1_{s}{ct}", [P, 512], F32)) for ct in range(2)] for s in range(2)]
        ps2 = [ctx.enter_context(nc.psum_tensor(f"ps2_{s}", [P, QS * C], F32)) for s in range(2)]

        consts_loaded = sem("consts_loaded")
        coef_ready = sem("coef_ready")
        dve_chain = sem("dve_chain")
        head_loaded = [sem(f"head_loaded{s}") for s in range(2)]
        last_loaded = [sem(f"last_loaded{s}") for s in range(2)]
        tail_loaded = [sem(f"tail_loaded{s}") for s in range(2)]
        head_used = sem("head_used")
        last_used = sem("last_used")
        stats_loaded = [sem(f"stats_loaded{s}") for s in range(2)]
        stats_used = [sem(f"stats_used{s}") for s in range(2)]
        resid_loaded = [sem(f"resid_loaded{s}") for s in range(RING)]
        stored = [sem(f"stored{s}") for s in range(RING)]
        hw_done = sem("hw_done")
        y1_ready = sem("y1_ready")
        c_done = sem("c_done")
        centred = sem("centred")
        summed = sem("summed")
        part_ready = sem("part_ready")
        part_summed = sem("part_summed")
        var_ready = sem("var_ready")
        std_ready = sem("std_ready")
        mean_lhs_ready = sem("mean_lhs_ready")
        means_done = sem("means_done")
        norm_ready = sem("norm_ready")

        m_c = coef[1][:, O_C:O_C + NC2]
        HEAD = range(0, 2 * TPU)
        TAIL = range(2 * TPU, TILES - 1)
        LAST = TILES - 1

        block = ctx.enter_context(nc.Block())

        @block.sync
        def _(sp):
            sp.dma_start(taps_sb[:, :, :], taps).then_inc(consts_loaded, 16)
            sp.dma_start(mask_sb[:, :, :], gmask).then_inc(consts_loaded, 16)
            sp.dma_start(h_sb[:, :], h.partition_broadcast(P)).then_inc(consts_loaded, 16)

            with sp.Fori(0, ST_TILES // 2) as i:
                for s in range(2):
                    sp.wait_ge(stats_used[s], i)
                    sp.dma_start(stats_in[s][:, :], x_stats[bass.ds(i * 2 + s, 1)].rearrange("o p f -> (o p) f")
                                 ).then_inc(stats_loaded[s], 16)

            def load_tiles(row, half, tiles, done):
                for hh in range(2):
                    for wi in range(WP):
                        p0 = hh * 64 + wi * 2 + half
                        sp.dma_start(strip[p0:p0 + 57:8, tiles.start:tiles.stop, :],
                                     x_strip[wi, bass.ds((row + hh * PAIRS) * 2, ROWS), tiles.start:tiles.stop, :]
                                     ).then_inc(done[half], 16)

            def load_last(row, half):
                for hh in range(2):
                    p0 = hh * 64 + half
                    sp.dma_start(strip[p0:p0 + 63:2, LAST, :],
                                 x_strip_t[LAST, bass.ds((row + hh * PAIRS) * 2, ROWS), :, :]
                                 ).then_inc(last_loaded[half], 16)

            def batch(b, ahead):
                sp.wait_ge(hw_done, b * (2 * UPB))
                before = b * H + (PAIRS - CP)
                load_tiles(before, 1, HEAD, head_loaded)
                load_last(before, 1)
                load_tiles(before, 1, TAIL, tail_loaded)
                with sp.Fori(0, CHUNKS // 2) as kk:
                    for j in range(2):
                        row = b * H + kk * (2 * CP) + j * CP
                        sp.wait_ge(head_used, b * CHUNKS + kk * 2 + j)
                        load_tiles(row, j, HEAD, head_loaded)
                        if ahead:
                            sp.wait_ge(stats_used[j], b * (CHUNKS // 2) + kk + CHUNKS // 2)
                            sp.dma_start(stats_in[j][:, :],
                                         x_stats[bass.ds(b * ST_TILES + kk * 2 + (ST_TILES + j), 1)].rearrange("o p f -> (o p) f")
                                         ).then_inc(stats_loaded[j], 16)
                        sp.wait_ge(last_used, b * CHUNKS + kk * 2 + j)
                        load_last(row, j)
                        for u in range(UNITS):
                            s = j * UNITS + u
                            sp.wait_ge(stored[s], b * (8 * CHUNKS) + kk * 16)
                            src = x_rows[bass.ds(b * H + kk * (2 * ROWS) + j * ROWS, ROWS), u * UW * C:(u + 1) * UW * C]
                            sp.dma_start(resid[s][:, :], src.rearrange("h (w f) -> w h f", w=16)
                                         ).then_inc(resid_loaded[s], 16)
                        sp.wait_ge(hw_done, b * (2 * UPB) + kk * (4 * UNITS) + j * 2 * UNITS)
                        load_tiles(row, j, TAIL, tail_loaded)

            with sp.Fori(0, B - 1) as b:
                batch(b, True)
            batch(B - 1, False)

        @block.gpsimd
        def _(pool):
            def centre(s, b, kk):
                pool.wait_ge(resid_loaded[s], b * (8 * CHUNKS) + kk * 16 + 16)
                r4 = resid[s][:, :].rearrange("p (n f) -> p n f", n=2)
                m4 = means_w3[:, :].rearrange("p (n f) -> p n f", n=1).broadcast_to([P, 2, 2 * C])
                nc.gpsimd.tensor_tensor(r4, r4, m4, ALU.add).then_inc(centred, 1)

            def store(s, b, kk):
                j, u = divmod(s, UNITS)
                pool.wait_ge(summed, b * UPB + kk * RING + (s + 3))
                dst = out_rows[bass.ds(b * H + kk * (2 * ROWS) + j * ROWS, ROWS), u * UW * C:(u + 1) * UW * C]
                pool.dma_start(dst.rearrange("h (w f) -> w h f", w=16), resid[s][:, :]).then_inc(stored[s], 16)

            with pool.Fori(0, B) as b:
                pool.wait_ge(norm_ready, b + 1)
                for s in range(UNITS):
                    centre(s, b, 0)
                with pool.Fori(0, CHUNKS // 2 - 1) as kk:
                    for s in range(RING):
                        if s < UNITS:
                            centre(s + UNITS, b, kk)
                        else:
                            centre(s - UNITS, b, kk + 1)
                        store(s, b, kk)
                for s in range(RING):
                    if s < UNITS:
                        centre(s + UNITS, b, CHUNKS // 2 - 1)
                    store(s, b, CHUNKS // 2 - 1)
            for s in range(RING):
                pool.wait_ge(stored[s], 16 * B * CHUNKS // 2)

        @block.tensor
        def _(pe):
            pe.wait_ge(coef_ready, 1)

            def rows_width(j, b, kk):
                phase, u = divmod(j, UNITS)
                first = u * TPU
                full = [(t, 0, N1, (t - first) * 2 * WP * ROWS) for t in range(first, first + TPU - 1)]
                edge = (first + TPU - 1, 0, 2 * WP * ROWS, (TPU - 1) * 2 * WP * ROWS)
                halo = ((first - 1) % TILES, 2 * WP * ROWS, N1, 0)

                def product(ct, what, start, stop):
                    t, a, z, at = what
                    return nc.tensor.matmul(ps1[j % 2][ct][:, at:at + z - a], strip[:, t, ct * P:(ct + 1) * P],
                                            m_hw[:, phase, a:z], start=start, stop=stop, skip_group_check=True)

                uses0 = b * (CHUNKS // 2) + kk
                uses = uses0 + 1 if phase == 0 else uses0 + b + 2
                if u == 0:
                    pe.wait_ge(head_loaded[phase], uses * (16 * 2 * WP))
                elif u == 2:
                    pe.wait_ge(tail_loaded[phase], uses * (16 * 2 * WP))
                if u == 0:
                    for ct in range(2):
                        for n, what in enumerate(full + [edge]):
                            product(ct, what, n == 0, False)
                    pe.wait_ge(last_loaded[phase], uses * 32)
                    for ct in range(2):
                        product(ct, halo, False, True).then_inc(hw_done, 1)
                    return
                lead, rest = (halo, full + [edge]) if u < 3 else (edge, [halo] + full)
                for ct in range(2):
                    mm = product(ct, lead, True, False)
                if u == 2:
                    mm.then_inc(head_used, 1)
                if u == 3:
                    mm.then_inc(last_used, 1)
                for ct in range(2):
                    for n, what in enumerate(rest):
                        mm = product(ct, what, False, n == len(rest) - 1)
                    mm.then_inc(hw_done, 1)

            def channels(j, b, kk):
                if j == 0:
                    pe.wait_ge(norm_ready, b + 1)
                pe.wait_ge(y1_ready, b * (2 * UPB) + kk * (2 * RING) + (2 * j + 2))
                pe.wait_ge(summed, b * UPB + kk * RING + (j + 1))
                for q in range(QS):
                    o = ps2[j % 2][:, q * C:(q + 1) * C]
                    data = [y1[j % 2][ct][:, q * P:(q + 1) * P] for ct in range(2)]
                    nc.tensor.matmul(o[:, 0:NC2], data[0], m_cr[:, 0, :], start=True, stop=False, skip_group_check=True)
                    nc.tensor.matmul(o[:, P:C], data[1], m_cr[:, 1, 0:P], start=False, stop=False, skip_group_check=True)
                    mm = nc.tensor.matmul(o[:, 0:HALO], data[1], m_cr[:, 1, P:NC2], start=False, stop=True,
                                          skip_group_check=True)
                mm.then_inc(c_done, 1)

            with pe.Fori(0, B) as b:
                pe.wait_ge(head_loaded[1], b * (16 * 2 * WP * (CHUNKS // 2 + 1)) + 16 * 2 * WP)
                pe.wait_ge(last_loaded[1], b * (32 * (CHUNKS // 2 + 1)) + 32)
                pe.wait_ge(tail_loaded[1], b * (16 * 2 * WP * (CHUNKS // 2 + 1)) + 16 * 2 * WP)
                rows_width(0, b, 0)
                pe.wait_ge(summed, b * UPB + 2)
                for n in range(2):
                    pe.wait_ge(part_ready, b * 2 + (n + 1))
                    nc.tensor.matmul(ps2[0][:, n * GROUPS:(n + 1) * GROUPS], ones[:, :], part[:, :], start=True, stop=True
                                     ).then_inc(part_summed, 1)
                pe.wait_ge(mean_lhs_ready, b + 1)
                for a in range(2):
                    o = ps2[1][:, a * C:(a + 1) * C]
                    nc.tensor.matmul(o[:, 0:NC2], mean_lhs[:, 0, a, :], m_c, start=True, stop=False, skip_group_check=True)
                    nc.tensor.matmul(o[:, P:C], mean_lhs[:, 1, a, :], m_c[:, 0:P], start=False, stop=False,
                                     skip_group_check=True)
                    mm = nc.tensor.matmul(o[:, 0:HALO], mean_lhs[:, 1, a, :], m_c[:, P:NC2], start=False, stop=True,
                                          skip_group_check=True)
                mm.then_inc(means_done, 1)
                with pe.Fori(0, CHUNKS // 2 - 1) as kk:
                    for j in range(RING):
                        if j < RING - 1:
                            rows_width(j + 1, b, kk)
                        else:
                            rows_width(0, b, kk + 1)
                        channels(j, b, kk)
                for j in range(RING):
                    if j < RING - 1:
                        rows_width(j + 1, b, CHUNKS // 2 - 1)
                    channels(j, b, CHUNKS // 2 - 1)

        @block.scalar
        def _(act):
            with act.Fori(0, B) as b:
                act.wait_ge(var_ready, b + 1)
                nc.scalar.activation(std_sb[:, :], var_sb[:, :], ACT.Sqrt).then_inc(std_ready, 1)
                with act.Fori(0, CHUNKS // 2) as kk:
                    for j in range(RING):
                        for ct in range(2):
                            act.wait_ge(hw_done, b * (2 * UPB) + kk * (2 * RING) + (2 * j + ct + 1))
                            for z in range(2):
                                src = ps1[j % 2][ct][64 * z:64 * z + 64, :]
                                dst = y1[j % 2][z][64 * ct:64 * ct + 64, :]
                                last = nc.scalar.activation(dst.rearrange("p (q w h) -> p q w h", q=QS, h=ROWS),
                                                            src.rearrange("p (w q h) -> p q w h", q=QS, h=ROWS),
                                                            ACT.Copy)
                            last.then_inc(y1_ready, 1)

        @block.vector
        def _(dve):
            count = [0]

            def link(ins):
                count[0] += 1
                ins.then_inc(dve_chain, 1)
                dve.wait_ge(dve_chain, count[0])

            dve.wait_ge(consts_loaded, 48)
            link(nc.vector.memset(ones[:, :], 1.0 / (2 * ST_TILES * P)))
            link(nc.vector.tensor_scalar(coef[0][:, :], taps_sb[:, 0, :], h_sb[:, 0:1], None, ALU.mult))
            for i in range(1, TAPS):
                link(nc.vector.scalar_tensor_tensor(out=coef[i % 2][:, :], in0=taps_sb[:, i, :], scalar=h_sb[:, i:i + 1],
                                                    in1=coef[(i + 1) % 2][:, :], op0=ALU.mult, op1=ALU.add))
            NW = 2 * WP + HALO
            for phase in range(2):
                a_w = coef[1][:, O_W:O_W + NW].rearrange("p (w o) -> p w o", o=1).broadcast_to([P, NW, ROWS])
                a_h = coef[1][:, O_H + phase * ROWS:O_H + (phase + 1) * ROWS].rearrange("p (o h) -> p o h", o=1
                                                                                        ).broadcast_to([P, NW, ROWS])
                link(nc.vector.tensor_tensor(m_hw[:, phase, :].rearrange("p (w h) -> p w h", h=ROWS), a_w, a_h, ALU.mult))
            for a in range(2):
                for e in range(2):
                    link(nc.vector.tensor_scalar(row_sums[:, a, e:P:2], ones[:, 0:P // 2], float(2 * ST_TILES * P),
                                                 coef[1][:, O_S + e:O_S + e + 1], ALU.mult, ALU.mult))
                link(nc.vector.tensor_scalar(row_sums[:, a, :], row_sums[:, a, :], coef[1][:, O_S + a:O_S + a + 1],
                                             None, ALU.mult))
            SETUP = count[0]
            nc.vector.memset(junk[:, :], 0.0).then_inc(coef_ready, 1)
            nc.vector.memset(dev[:, 0, 0, :], 0.0).then_inc(summed, 2)

            def group_stats(s, k, g0, g1, loads, last):
                if g0 == 0:
                    dve.wait_ge(stats_loaded[s], loads)
                view = stats_in[s][:, :].rearrange("p (s c) -> p s c", c=C)
                for g in range(g0, g1):
                    ins = nc.vector.bn_stats(records[:, bass.ds(k, 1), g, :].rearrange("p o f -> p (o f)"),
                                             view[:, :, g * GC:(g + 1) * GC])
                if last:
                    ins.then_inc(stats_used[s], 1)

            def finish_stats(b):
                n = [0]
                CHAIN = 13

                def link(ins):
                    n[0] += 1
                    ins.then_inc(dve_chain, 1)
                    dve.wait_ge(dve_chain, b * CHAIN + (SETUP + n[0]))

                for s in range(2):
                    dve.wait_ge(stats_used[s], b * (CHUNKS // 2) + CHUNKS // 2)
                rec = records[:, :, :, :].rearrange("p k g (s r) -> p r k g s", r=3)
                means, sq = rec[:, 1], rec[:, 2]
                nc.vector.tensor_reduce(part[:, :], means.rearrange("p k g s -> p g k s"), AX.XY, ALU.add
                                        ).then_inc(part_ready, 1)
                dve.wait_ge(part_summed, b * 2 + 1)
                link(nc.vector.tensor_copy(gstat[:, 0, :], ps2[0][:, 0:GROUPS]))
                mean_b = gstat[:, 0:1, :].rearrange("p o (g e) -> p o g e", e=1).broadcast_to([P, ST_TILES, GROUPS, 2])
                link(nc.vector.tensor_tensor(dev[:, :, :, :], means, mean_b, ALU.subtract))
                d1, d2 = (v[:, :, :, :].rearrange("p k g s -> p (k g s)") for v in (dev, dev2))
                link(nc.vector.scalar_tensor_tensor(out=d2, in0=d1, scalar=float(POS * GC // 2), in1=d1,
                                                    op0=ALU.mult, op1=ALU.mult))
                link(nc.vector.tensor_tensor(dev[:, :, :, :], dev2[:, :, :, :], sq, ALU.add))
                nc.vector.tensor_reduce(part[:, :], dev[:, :, :, :].rearrange("p k g s -> p g k s"), AX.XY, ALU.add
                                        ).then_inc(part_ready, 1)
                dve.wait_ge(part_summed, b * 2 + 2)
                nc.vector.tensor_scalar(var_sb[:, :], ps2[0][:, GROUPS:2 * GROUPS], 2.0 / (POS * GC), EPS,
                                        ALU.mult, ALU.add).then_inc(var_ready, 1)
                dve.wait_ge(std_ready, b + 1)
                link(nc.vector.reciprocal(gstat[:, 1, :], std_sb[:, :]))
                for ct in range(2):
                    for v in range(2):
                        link(nc.vector.tensor_tensor_reduce(junk[:, :], gstat[:, v, :], mask_sb[:, ct, :], 1.0, 0.0,
                                                            ALU.mult, ALU.add, chan[:, ct, v:v + 1]))
                    link(nc.vector.scalar_tensor_tensor(out=neg_mr[:, ct:ct + 1], in0=chan[:, ct, 0:1], scalar=-1.0,
                                                        in1=chan[:, ct, 1:2], op0=ALU.mult, op1=ALU.mult))
                    for a in range(2):
                        ins = nc.vector.tensor_scalar(mean_lhs[:, ct, a, :], row_sums[:, a, :], neg_mr[:, ct:ct + 1],
                                                      None, ALU.mult)
                    link(nc.vector.tensor_scalar(m_cr[:, ct, :], m_c, chan[:, ct, 1:2], None, ALU.mult))
                nc.vector.memset(junk[:, 1:2], 0.0).then_inc(mean_lhs_ready, 1)
                dve.wait_ge(means_done, b + 1)
                nc.vector.tensor_copy(means_w3[:, :], ps2[1][:, 0:2 * C]).then_inc(norm_ready, 1)
                assert n[0] == CHAIN

            with dve.Fori(0, ST_TILES // 2) as i:
                for s in range(2):
                    group_stats(s, i * 2 + s, 0, GROUPS, i * 16 + 16, True)

            def batch(b, ahead):
                finish_stats(b)
                with dve.Fori(0, CHUNKS // 2) as kk:
                    for s in range(RING):
                        j, u = divmod(s, UNITS)
                        dve.wait_ge(c_done, b * UPB + kk * RING + (s + 1))
                        dve.wait_ge(centred, b * UPB + kk * RING + (s + 1))
                        nc.vector.tensor_tensor(resid[s][:, :], ps2[s % 2][:, :], resid[s][:, :], ALU.add
                                                ).then_inc(summed, 1)
                        if ahead:
                            group_stats(j, kk * 2 + j, u * GC, (u + 1) * GC,
                                        b * (8 * CHUNKS) + kk * 16 + (8 * CHUNKS + 16), u == UNITS - 1)

            with dve.Fori(0, B - 1) as b:
                batch(b, True)
            batch(B - 1, False)


def kernel(**inputs):
    import numpy as _np
    import concourse.bacc as _bacc
    from concourse import mybir as _mybir
    from concourse.bass_utils import run_bass_kernel_spmd as _run

    nc = _bacc.Bacc("TRN2", target_bir_lowering=False, num_devices=1)
    arrays, args = {}, []
    host = {"x": inputs["x"], "L0_conv_h": inputs["L0_conv_h"], "taps": tap_table(), "gmask": group_masks()}
    for name, a in host.items():
        a = _np.ascontiguousarray(a)
        arrays[f"in_{name}_dram"] = a
        args.append(nc.dram_tensor(f"in_{name}_dram", a.shape, _mybir.dt.from_np(a.dtype), kind="ExternalInput").ap())
    args.append(nc.dram_tensor("out_0_dram", (B, H, W, C), _mybir.dt.from_np(_np.dtype("float32")),
                               kind="ExternalOutput").ap())
    wavelet_preact_kernel(nc, *args)
    r = _run(nc, [arrays], core_ids=[0])
    return r.results[0]["out_0_dram"]
```

```python
from contextlib import ExitStack

import numpy as np

import concourse.bass as bass
from concourse import mybir

P = 128
B, H, W, C = 4, 256, 256, 256
PAIRS = 128
TAPS = 8
GROUPS = 32
GC = C // GROUPS
EPS = 1e-5

CP = 4
CHUNKS = PAIRS // CP
ROWS = 2 * CP
WP = 4
TILES = PAIRS // WP
UNITS = 4
TPU = TILES // UNITS
UW = W // UNITS
HALO = TAPS - 2
N1 = (2 * WP + HALO) * ROWS
NC2 = P + HALO
RING = 8
QS = 4
POS = 32
PIECES = 4
ST_TILES = H * W // (P * POS)
UPB = CHUNKS * UNITS
FREE = 1
SLOTS = 2
SHARE = [0, 5, 5, 5, 5, 4, 4, 4]
assert 2 * ST_TILES == CHUNKS and 2 * UNITS == RING and sum(SHARE) == GROUPS

O_H, O_W = 0, 2 * ROWS
O_C = O_W + 2 * WP + HALO
O_S = O_C + NC2
NCOEF = O_S + 2

F32 = mybir.dt.float32
ALU = mybir.AluOpType
ACT = mybir.ActivationFunctionType
AX = mybir.AxisListType


def tap_table():
    t = np.zeros((P, TAPS, NCOEF), np.float32)

    def put(p, col, high, d):
        if 0 <= d < TAPS:
            if high:
                t[p, TAPS - 1 - d, col] = 1.0 if d % 2 == 0 else -1.0
            else:
                t[p, d, col] = 1.0

    for p in range(P):
        strip, rest = p % 2, p // 2
        hh, hi, wh, wi = rest // 32, rest // 8 % 4, rest // 4 % 2, rest % 4
        for phase in range(2):
            for n in range(ROWS):
                put(p, O_H + phase * ROWS + n, hh, n - 2 * hi + (0 if strip == phase else ROWS))
        for n in range(2 * WP + HALO):
            put(p, O_W + n, wh, n - 2 * wi)
        for n in range(NC2):
            put(p, O_C + n, p // 64, n - 2 * (p % 64))
    for i in range(TAPS):
        t[:, i, O_S] = 1.0
        t[:, i, O_S + 1] = 1.0 if i % 2 else -1.0
    return t


def group_masks():
    m = np.zeros((P, 2, GROUPS), np.float32)
    for ct in range(2):
        for p in range(P):
            c = (0 if p < 64 else 128) + 64 * ct + p % 64
            m[p, ct, c // GC] = 1.0
    return m


def wavelet_preact_kernel(nc, x, h, taps, gmask, out):
    x_rows = x.rearrange("b h w c -> (b h) (w c)")
    out_rows = out.rearrange("b h w c -> (b h) (w c)")
    x_strip = x.rearrange("b h (v t i) c -> i (b h v) t c", v=2, i=WP)
    x_strip_t = x.rearrange("b h (v t i) c -> t (b h v) i c", v=2, i=WP)
    x_stats = x.rearrange("b h w c -> (b h w c)").rearrange("(n p f) -> n p f", p=P, f=POS * C)

    with ExitStack() as ctx:
        def sb(name, shape):
            return ctx.enter_context(nc.sbuf_tensor(name, shape, F32))

        def sem(name):
            return ctx.enter_context(nc.semaphore(name))

        strip = sb("strip", [P, TILES, C])
        stats_in = [sb(f"stats_in{s}", [P, POS * C]) for s in range(2)]
        resid = [sb(f"resid{s}", [P, QS * C]) for s in range(RING)]
        y1 = [[sb(f"y1_{s}{ct}", [P, UW * ROWS]) for ct in range(2)] for s in range(2)]
        records = sb("records", [P, ST_TILES, GROUPS, 6])
        dev = sb("dev", [P, ST_TILES, GROUPS, 2])
        dev2 = sb("dev2", [P, ST_TILES, GROUPS, 2])
        taps_sb = sb("taps_sb", [P, TAPS, NCOEF])
        mask_sb = sb("mask_sb", [P, 2, GROUPS])
        h_sb = sb("h_sb", [P, TAPS])
        coef = [sb(f"coef{s}", [P, NCOEF]) for s in range(2)]
        m_hw = sb("m_hw", [P, 2, N1])
        ones = sb("ones", [P, P])
        part = sb("part", [P, GROUPS])
        gstat = sb("gstat", [P, 2, GROUPS])
        var_sb = sb("var_sb", [P, GROUPS])
        std_sb = sb("std_sb", [P, GROUPS])
        junk = sb("junk", [P, GROUPS])
        chan = sb("chan", [P, 2, 2])
        neg_mr = sb("neg_mr", [P, 2])
        row_sums = sb("row_sums", [P, 2, P])
        mean_lhs = sb("mean_lhs", [P, 2, 2, P])
        m_cr = sb("m_cr", [P, 2, NC2])
        means_w3 = sb("means_w3", [P, 2 * C])

        ps1 = [[ctx.enter_context(nc.psum_tensor(f"ps1_{s}{ct}", [P, 512], F32)) for ct in range(2)] for s in range(2)]
        ps2 = [ctx.enter_context(nc.psum_tensor(f"ps2_{s}", [P, 2, 512], F32)) for s in range(2)]

        consts_loaded = sem("consts_loaded")
        coef_ready = sem("coef_ready")
        dve_chain = sem("dve_chain")
        head_loaded = [sem(f"head_loaded{s}") for s in range(2)]
        last_loaded = [sem(f"last_loaded{s}") for s in range(2)]
        tail_loaded = [sem(f"tail_loaded{s}") for s in range(2)]
        head_used = sem("head_used")
        last_used = sem("last_used")
        stats_loaded = [sem(f"stats_loaded{s}") for s in range(2)]
        stats_used = [sem(f"stats_used{s}") for s in range(2)]
        resid_loaded = [sem(f"resid_loaded{s}") for s in range(RING)]
        stored = [sem(f"stored{s}") for s in range(RING)]
        hw_done = sem("hw_done")
        y1_ready = sem("y1_ready")
        c_done = sem("c_done")
        centred = sem("centred")
        wrapped = sem("wrapped")
        summed = sem("summed")
        part_ready = sem("part_ready")
        part_summed = sem("part_summed")
        var_ready = sem("var_ready")
        std_ready = sem("std_ready")
        mean_lhs_ready = sem("mean_lhs_ready")
        means_done = sem("means_done")
        norm_ready = sem("norm_ready")

        m_c = coef[1][:, O_C:O_C + NC2]
        HEAD = range(0, 2 * TPU)
        TAIL = range(2 * TPU, TILES - 1)
        LAST = TILES - 1

        block = ctx.enter_context(nc.Block())

        @block.sync
        def _(sp):
            sp.dma_start(taps_sb[:, :, :], taps).then_inc(consts_loaded, 16)
            sp.dma_start(mask_sb[:, :, :], gmask).then_inc(consts_loaded, 16)
            sp.dma_start(h_sb[:, :], h.partition_broadcast(P)).then_inc(consts_loaded, 16)

            for free in [hw_done, head_used, last_used] + stats_used:
                sp.sem_inc(free, FREE)

            def load_stats(tile, s, piece, uses):
                if piece == 0:
                    sp.wait_ge(stats_used[s], uses)
                n = POS * C // PIECES
                sp.dma_start(stats_in[s][:, piece * n:(piece + 1) * n],
                             x_stats[bass.ds(tile, 1), :, piece * n:(piece + 1) * n].rearrange("o p f -> (o p) f")
                             ).then_inc(stats_loaded[s], 16)

            with sp.Fori(0, ST_TILES // 2) as i:
                for s in range(2):
                    for piece in range(PIECES):
                        load_stats(i * 2 + s, s, piece, i + FREE)
            for piece in range(2):
                load_stats(ST_TILES, 0, piece, ST_TILES // 2 + FREE)

            def load_tiles(row, half, tiles, done):
                for hh in range(2):
                    for wi in range(WP):
                        p0 = hh * 64 + wi * 2 + half
                        sp.dma_start(strip[p0:p0 + 57:8, tiles.start:tiles.stop, :],
                                     x_strip[wi, bass.ds((row + hh * PAIRS) * 2, ROWS), tiles.start:tiles.stop, :]
                                     ).then_inc(done[half], 16)

            def load_last(row, half):
                for hh in range(2):
                    p0 = hh * 64 + half
                    sp.dma_start(strip[p0:p0 + 63:2, LAST, :],
                                 x_strip_t[LAST, bass.ds((row + hh * PAIRS) * 2, ROWS), :, :]
                                 ).then_inc(last_loaded[half], 16)

            def four_chunks(b, i, stats_now, stats_next, start=False):
                before = b * H + (PAIRS - CP)
                for c in range(4):
                    pair, j = divmod(c, 2)
                    row = b * H + i * (4 * CP) + c * CP

                    def load_resid(u):
                        s = j * UNITS + u
                        if not (start and pair == 0 and isinstance(b, int) and b == 0):
                            sp.wait_ge(stored[s], b * (8 * CHUNKS) + i * 32 + pair * 16)
                        src = x_rows[bass.ds(b * H + i * (4 * ROWS) + c * ROWS, ROWS), u * UW * C:(u + 1) * UW * C]
                        sp.dma_start(resid[s][:, :], src.rearrange("h (w f) -> w h f", w=16)
                                     ).then_inc(resid_loaded[s], 16)

                    def load_piece(half):
                        if j == 0 and stats_now:
                            load_stats(b * ST_TILES + i * 2 + (ST_TILES + pair), pair, 2 + half, None)
                        if j == 1 and stats_next[pair]:
                            load_stats(b * ST_TILES + i * 2 + (ST_TILES + pair + 1), 1 - pair, half,
                                       b * (ST_TILES // 2) + i + (ST_TILES // 2 + pair + FREE))

                    for u in range(2):
                        load_resid(u)
                    sp.wait_ge(head_used, b * CHUNKS + i * 4 + (c + FREE))
                    if start and c == 0:
                        load_tiles(before, 1, HEAD, head_loaded)
                    load_tiles(row, j, HEAD, head_loaded)
                    load_piece(0)
                    load_resid(2)
                    sp.wait_ge(last_used, b * CHUNKS + i * 4 + (c + FREE))
                    if start and c == 0:
                        load_last(before, 1)
                    load_last(row, j)
                    load_resid(3)
                    sp.wait_ge(hw_done, b * (2 * UPB) + i * (8 * UNITS) + (c * 2 * UNITS + FREE))
                    if start and c == 0:
                        load_tiles(before, 1, TAIL, tail_loaded)
                    load_tiles(row, j, TAIL, tail_loaded)
                    load_piece(1)

            four_chunks(0, 0, True, (True, True), start=True)
            with sp.Fori(1, CHUNKS // 4) as i:
                four_chunks(0, i, True, (True, True))
            with sp.Fori(1, B - 2) as b:
                four_chunks(b, 0, True, (True, True), start=True)
                with sp.Fori(1, CHUNKS // 4) as i:
                    four_chunks(b, i, True, (True, True))
            four_chunks(B - 2, 0, True, (True, True), start=True)
            with sp.Fori(1, CHUNKS // 4 - 1) as i:
                four_chunks(B - 2, i, True, (True, True))
            four_chunks(B - 2, CHUNKS // 4 - 1, True, (True, False))
            four_chunks(B - 1, 0, False, (False, False), start=True)
            with sp.Fori(1, CHUNKS // 4) as i:
                four_chunks(B - 1, i, False, (False, False))

        @block.gpsimd
        def _(pool):
            def centre(s, b, kk):
                pool.wait_ge(resid_loaded[s], b * (8 * CHUNKS) + kk * 16 + 16)
                r4 = resid[s][:, :].rearrange("p (n f) -> p n f", n=2)
                m4 = means_w3[:, :].rearrange("p (n f) -> p n f", n=1).broadcast_to([P, 2, 2 * C])
                nc.gpsimd.tensor_tensor(r4, r4, m4, ALU.add).then_inc(centred, 1)

            def store(s, b, kk):
                j, u = divmod(s, UNITS)
                pool.wait_ge(summed, b * (2 * UPB) + kk * (2 * RING) + (2 * s + 2 + SLOTS))
                dst = out_rows[bass.ds(b * H + kk * (2 * ROWS) + j * ROWS, ROWS), u * UW * C:(u + 1) * UW * C]
                pool.dma_start(dst.rearrange("h (w f) -> w h f", w=16), resid[s][:, :]).then_inc(stored[s], 16)

            with pool.Fori(0, B) as b:
                pool.wait_ge(norm_ready, b + 1)
                for s in range(UNITS):
                    centre(s, b, 0)
                with pool.Fori(0, CHUNKS // 2 - 1) as kk:
                    for s in range(RING):
                        if s < UNITS:
                            centre(s + UNITS, b, kk)
                        else:
                            centre(s - UNITS, b, kk + 1)
                        store(s, b, kk)
                for s in range(RING):
                    if s < UNITS:
                        centre(s + UNITS, b, CHUNKS // 2 - 1)
                    store(s, b, CHUNKS // 2 - 1)
            for s in range(RING):
                pool.wait_ge(stored[s], 16 * B * CHUNKS // 2)

        @block.tensor
        def _(pe):
            pe.wait_ge(coef_ready, 1)

            def rows_width(j, b, kk):
                phase, u = divmod(j, UNITS)
                first = u * TPU
                full = [(t, 0, N1, (t - first) * 2 * WP * ROWS) for t in range(first, first + TPU - 1)]
                edge = (first + TPU - 1, 0, 2 * WP * ROWS, (TPU - 1) * 2 * WP * ROWS)
                halo = ((first - 1) % TILES, 2 * WP * ROWS, N1, 0)

                def product(ct, what, start, stop):
                    t, a, z, at = what
                    return nc.tensor.matmul(ps1[j % 2][ct][:, at:at + z - a], strip[:, t, ct * P:(ct + 1) * P],
                                            m_hw[:, phase, a:z], start=start, stop=stop, skip_group_check=True)

                even = b * (CHUNKS // 2) + kk + 1
                odd = b * (CHUNKS // 2 + 1) + kk + (1 if phase == 0 else 2)

                def strips_in(loaded, per_strip):
                    if phase == 0:
                        pe.wait_ge(loaded[0], even * per_strip)
                    pe.wait_ge(loaded[1], odd * per_strip)

                if u == 0:
                    strips_in(head_loaded, 16 * 2 * WP)
                elif u == 2:
                    strips_in(tail_loaded, 16 * 2 * WP)
                if u == 0:
                    for ct in range(2):
                        for n, what in enumerate(full + [edge]):
                            product(ct, what, n == 0, False)
                    strips_in(last_loaded, 32)
                    for ct in range(2):
                        product(ct, halo, False, True).then_inc(hw_done, 1)
                    return
                lead, rest = (halo, full + [edge]) if u < 3 else (edge, [halo] + full)
                for ct in range(2):
                    mm = product(ct, lead, True, False)
                if u == 2:
                    mm.then_inc(head_used, 1)
                if u == 3:
                    mm.then_inc(last_used, 1)
                for ct in range(2):
                    for n, what in enumerate(rest):
                        mm = product(ct, what, False, n == len(rest) - 1)
                    mm.then_inc(hw_done, 1)

            def channel_product(o, data, m):
                nc.tensor.matmul(o[:, 0:NC2], data[0], m[0], start=True, stop=False, skip_group_check=True)
                return nc.tensor.matmul(o[:, P:P + NC2], data[1], m[1], start=False, stop=True, skip_group_check=True)

            def channels(j, b, kk):
                if j == 0:
                    pe.wait_ge(norm_ready, b + 1)
                pe.wait_ge(y1_ready, b * (2 * UPB) + kk * (2 * RING) + (2 * j + 2))
                for half in range(SLOTS):
                    pe.wait_ge(summed, b * (2 * UPB) + kk * (2 * RING) + (2 * j + half + 1))
                    for n in range(2):
                        q = 2 * half + n
                        mm = channel_product(ps2[half][:, n, :],
                                             [y1[j % 2][ct][:, q * P:(q + 1) * P] for ct in range(2)],
                                             [m_cr[:, ct, :] for ct in range(2)])
                    mm.then_inc(c_done, 1)

            with pe.Fori(0, B) as b:
                rows_width(0, b, 0)
                pe.wait_ge(summed, b * (2 * UPB) + SLOTS)
                for n in range(2):
                    pe.wait_ge(part_ready, b * 2 + (n + 1))
                    nc.tensor.matmul(ps2[0][:, 0, n * GROUPS:(n + 1) * GROUPS], ones[:, :], part[:, :], start=True, stop=True
                                     ).then_inc(part_summed, 1)
                pe.wait_ge(mean_lhs_ready, b + 1)
                for a in range(2):
                    mm = channel_product(ps2[1][:, a, :], [mean_lhs[:, ct, a, :] for ct in range(2)], [m_c, m_c])
                mm.then_inc(means_done, 1)
                with pe.Fori(0, CHUNKS // 2 - 1) as kk:
                    for j in range(RING):
                        if j < RING - 1:
                            rows_width(j + 1, b, kk)
                        else:
                            rows_width(0, b, kk + 1)
                        channels(j, b, kk)
                for j in range(RING):
                    if j < RING - 1:
                        rows_width(j + 1, b, CHUNKS // 2 - 1)
                    channels(j, b, CHUNKS // 2 - 1)

        @block.scalar
        def _(act):
            with act.Fori(0, B) as b:
                act.wait_ge(var_ready, b + 1)
                nc.scalar.activation(std_sb[:, :], var_sb[:, :], ACT.Sqrt).then_inc(std_ready, 1)
                with act.Fori(0, CHUNKS // 2) as kk:
                    for j in range(RING):
                        for ct in range(2):
                            act.wait_ge(hw_done, b * (2 * UPB) + kk * (2 * RING) + (2 * j + ct + 1 + FREE))
                            for z in range(2):
                                src = ps1[j % 2][ct][64 * z:64 * z + 64, :]
                                dst = y1[j % 2][z][64 * ct:64 * ct + 64, :]
                                last = nc.scalar.activation(dst.rearrange("p (q w h) -> p q w h", q=QS, h=ROWS),
                                                            src.rearrange("p (w q h) -> p q w h", q=QS, h=ROWS),
                                                            ACT.Copy)
                            last.then_inc(y1_ready, 1)

        @block.vector
        def _(dve):
            count = [0]

            def link(ins):
                count[0] += 1
                ins.then_inc(dve_chain, 1)
                dve.wait_ge(dve_chain, count[0])

            dve.wait_ge(consts_loaded, 48)
            link(nc.vector.memset(ones[:, :], 1.0 / (2 * ST_TILES * P)))
            link(nc.vector.tensor_scalar(coef[0][:, :], taps_sb[:, 0, :], h_sb[:, 0:1], None, ALU.mult))
            for i in range(1, TAPS):
                link(nc.vector.scalar_tensor_tensor(out=coef[i % 2][:, :], in0=taps_sb[:, i, :], scalar=h_sb[:, i:i + 1],
                                                    in1=coef[(i + 1) % 2][:, :], op0=ALU.mult, op1=ALU.add))
            NW = 2 * WP + HALO
            for phase in range(2):
                a_w = coef[1][:, O_W:O_W + NW].rearrange("p (w o) -> p w o", o=1).broadcast_to([P, NW, ROWS])
                a_h = coef[1][:, O_H + phase * ROWS:O_H + (phase + 1) * ROWS].rearrange("p (o h) -> p o h", o=1
                                                                                        ).broadcast_to([P, NW, ROWS])
                link(nc.vector.tensor_tensor(m_hw[:, phase, :].rearrange("p (w h) -> p w h", h=ROWS), a_w, a_h, ALU.mult))
            for a in range(2):
                for e in range(2):
                    link(nc.vector.tensor_scalar(row_sums[:, a, e:P:2], ones[:, 0:P // 2], float(2 * ST_TILES * P),
                                                 coef[1][:, O_S + e:O_S + e + 1], ALU.mult, ALU.mult))
                link(nc.vector.tensor_scalar(row_sums[:, a, :], row_sums[:, a, :], coef[1][:, O_S + a:O_S + a + 1],
                                             None, ALU.mult))
            SETUP = count[0]
            nc.vector.memset(junk[:, :], 0.0).then_inc(coef_ready, 1)
            nc.vector.memset(dev[:, 0, 0, :], 0.0).then_inc(summed, SLOTS)

            def group_stats(s, k, g0, g1, loads, last):
                if g0 == 0:
                    dve.wait_ge(stats_loaded[s], loads)
                view = stats_in[s][:, :].rearrange("p (s c) -> p s c", c=C)
                for g in range(g0, g1):
                    ins = nc.vector.bn_stats(records[:, bass.ds(k, 1), g, :].rearrange("p o f -> p (o f)"),
                                             view[:, :, g * GC:(g + 1) * GC])
                if last:
                    ins.then_inc(stats_used[s], 1)

            def finish_stats(b):
                n = [0]
                CHAIN = 18

                def link(ins):
                    n[0] += 1
                    ins.then_inc(dve_chain, 1)
                    dve.wait_ge(dve_chain, b * CHAIN + (SETUP + n[0]))

                for s in range(2):
                    dve.wait_ge(stats_used[s], b * (ST_TILES // 2) + (ST_TILES // 2 + FREE))
                rec = records[:, :, :, :].rearrange("p k g (s r) -> p r k g s", r=3)
                means, sq = rec[:, 1], rec[:, 2]
                nc.vector.tensor_reduce(part[:, :], means.rearrange("p k g s -> p g k s"), AX.XY, ALU.add
                                        ).then_inc(part_ready, 1)
                dve.wait_ge(part_summed, b * 2 + 1)
                link(nc.vector.tensor_copy(gstat[:, 0, :], ps2[0][:, 0, 0:GROUPS]))
                mean_b = gstat[:, 0:1, :].rearrange("p o (g e) -> p o g e", e=1).broadcast_to([P, ST_TILES, GROUPS, 2])
                link(nc.vector.tensor_tensor(dev[:, :, :, :], means, mean_b, ALU.subtract))
                d1, d2 = (v[:, :, :, :].rearrange("p k g s -> p (k g s)") for v in (dev, dev2))
                link(nc.vector.scalar_tensor_tensor(out=d2, in0=d1, scalar=float(POS * GC // 2), in1=d1,
                                                    op0=ALU.mult, op1=ALU.mult))
                link(nc.vector.tensor_tensor(dev[:, :, :, :], dev2[:, :, :, :], sq, ALU.add))
                nc.vector.tensor_reduce(part[:, :], dev[:, :, :, :].rearrange("p k g s -> p g k s"), AX.XY, ALU.add
                                        ).then_inc(part_ready, 1)
                dve.wait_ge(part_summed, b * 2 + 2)
                nc.vector.tensor_scalar(var_sb[:, :], ps2[0][:, 0, GROUPS:2 * GROUPS], 2.0 / (POS * GC), EPS,
                                        ALU.mult, ALU.add).then_inc(var_ready, 1)
                dve.wait_ge(std_ready, b + 1)
                r0, vr, r = std_sb[:, :], junk[:, :], gstat[:, 1, :]
                link(nc.vector.reciprocal(r0, std_sb[:, :]))
                link(nc.vector.tensor_tensor(vr, var_sb[:, :], r0, ALU.mult))
                link(nc.vector.tensor_tensor(vr, vr, r0, ALU.mult))
                link(nc.vector.tensor_scalar(vr, vr, -0.5, 1.5, ALU.mult, ALU.add))
                link(nc.vector.tensor_tensor(r, r0, vr, ALU.mult))
                for ct in range(2):
                    for v in range(2):
                        link(nc.vector.tensor_tensor_reduce(junk[:, :], gstat[:, v, :], mask_sb[:, ct, :], 1.0, 0.0,
                                                            ALU.mult, ALU.add, chan[:, ct, v:v + 1]))
                    link(nc.vector.scalar_tensor_tensor(out=neg_mr[:, ct:ct + 1], in0=chan[:, ct, 0:1], scalar=-1.0,
                                                        in1=chan[:, ct, 1:2], op0=ALU.mult, op1=ALU.mult))
                    for a in range(2):
                        ins = nc.vector.tensor_scalar(mean_lhs[:, ct, a, :], row_sums[:, a, :], neg_mr[:, ct:ct + 1],
                                                      None, ALU.mult)
                    link(nc.vector.tensor_scalar(m_cr[:, ct, :], m_c, chan[:, ct, 1:2], None, ALU.mult))
                nc.vector.memset(junk[:, 1:2], 0.0).then_inc(mean_lhs_ready, 1)
                dve.wait_ge(means_done, b + 1)
                w3 = means_w3[:, :].rearrange("p (a c) -> p a c", c=C)
                link(nc.vector.tensor_copy(w3, ps2[1][:, :, 0:C]))
                nc.vector.tensor_tensor(w3[:, :, 0:HALO], ps2[1][:, :, C:C + HALO], w3[:, :, 0:HALO], ALU.add
                                        ).then_inc(norm_ready, 1)
                assert n[0] == CHAIN

            with dve.Fori(0, ST_TILES // 2) as i:
                for s in range(2):
                    group_stats(s, i * 2 + s, 0, GROUPS, i * (16 * PIECES) + 16 * PIECES, True)

            def batch(b, ahead):
                finish_stats(b)
                with dve.Fori(0, CHUNKS // 4) as i:
                    for unit in range(2 * RING):
                        pair, s = divmod(unit, RING)
                        dve.wait_ge(centred, b * UPB + i * (2 * RING) + (unit + 1))
                        for half in range(SLOTS):
                            r = resid[s][:, half * 2 * C:(half + 1) * 2 * C].rearrange("p (q c) -> p q c", c=C)
                            count_halves = b * (2 * UPB) + i * (4 * RING) + (2 * unit + half + 1)
                            dve.wait_ge(c_done, count_halves)
                            nc.vector.tensor_tensor(r[:, :, 0:HALO], ps2[half][:, :, C:C + HALO], r[:, :, 0:HALO], ALU.add
                                                    ).then_inc(wrapped, 1)
                            dve.wait_ge(wrapped, count_halves)
                            nc.vector.tensor_tensor(r, ps2[half][:, :, 0:C], r, ALU.add).then_inc(summed, 1)
                        if ahead and SHARE[s]:
                            g0 = sum(SHARE[:s])
                            group_stats(pair, i * 2 + pair, g0, g0 + SHARE[s],
                                        b * (8 * PIECES * ST_TILES) + i * (16 * PIECES)
                                        + 16 * PIECES * (ST_TILES // 2 + 1), s == RING - 1)

            with dve.Fori(0, B - 1) as b:
                batch(b, True)
            batch(B - 1, False)


def kernel(**inputs):
    import numpy as _np
    import concourse.bacc as _bacc
    from concourse import mybir as _mybir
    from concourse.bass_utils import run_bass_kernel_spmd as _run

    nc = _bacc.Bacc("TRN2", target_bir_lowering=False, num_devices=1)
    arrays, args = {}, []
    host = {"x": inputs["x"], "L0_conv_h": inputs["L0_conv_h"], "taps": tap_table(), "gmask": group_masks()}
    for name, a in host.items():
        a = _np.ascontiguousarray(a)
        arrays[f"in_{name}_dram"] = a
        args.append(nc.dram_tensor(f"in_{name}_dram", a.shape, _mybir.dt.from_np(a.dtype), kind="ExternalInput").ap())
    args.append(nc.dram_tensor("out_0_dram", (B, H, W, C), _mybir.dt.from_np(_np.dtype("float32")),
                               kind="ExternalOutput").ap())
    wavelet_preact_kernel(nc, *args)
    r = _run(nc, [arrays], core_ids=[0])
    return r.results[0]["out_0_dram"]
```

```python
from contextlib import ExitStack

import numpy as np

import concourse.bass as bass
from concourse import mybir

P = 128
B, H, W, C = 4, 256, 256, 256
PAIRS = 128
TAPS = 8
GROUPS = 32
GC = C // GROUPS
EPS = 1e-5

CP = 4
CHUNKS = PAIRS // CP
ROWS = 2 * CP
WP = 4
TILES = PAIRS // WP
UNITS = 4
TPU = TILES // UNITS
UW = W // UNITS
HALO = TAPS - 2
N1 = (2 * WP + HALO) * ROWS
NC2 = P + HALO
RING = 8
QS = 4
POS = 32
PIECES = 4
ST_TILES = H * W // (P * POS)
UPB = CHUNKS * UNITS
FREE = 1
SLOTS = 2
SHARE = [0, 5, 5, 5, 5, 5, 5, 2]
USES = [ST_TILES // 2, ST_TILES // 2 - 1]
FIRST_USES = (ST_TILES - 1) // 3
FIRST_ORDER = (2, 0, 1)
assert 3 * FIRST_USES == ST_TILES - 1 and ROWS * W * 2 == P * POS and 2 * ST_TILES == CHUNKS and 2 * UNITS == RING and sum(SHARE) == GROUPS

O_H, O_W = 0, 2 * ROWS
O_C = O_W + 2 * WP + HALO
O_S = O_C + NC2
NCOEF = O_S + 2

F32 = mybir.dt.float32
ALU = mybir.AluOpType
ACT = mybir.ActivationFunctionType
AX = mybir.AxisListType


def tap_table():
    t = np.zeros((P, TAPS, NCOEF), np.float32)

    def put(p, col, high, d):
        if 0 <= d < TAPS:
            if high:
                t[p, TAPS - 1 - d, col] = 1.0 if d % 2 == 0 else -1.0
            else:
                t[p, d, col] = 1.0

    for p in range(P):
        strip, rest = p % 2, p // 2
        hh, hi, wh, wi = rest // 32, rest // 8 % 4, rest // 4 % 2, rest % 4
        for phase in range(2):
            for n in range(ROWS):
                put(p, O_H + phase * ROWS + n, hh, n - 2 * hi + (0 if strip == phase else ROWS))
        for n in range(2 * WP + HALO):
            put(p, O_W + n, wh, n - 2 * wi)
        for n in range(NC2):
            put(p, O_C + n, p // 64, n - 2 * (p % 64))
    for i in range(TAPS):
        t[:, i, O_S] = 1.0
        t[:, i, O_S + 1] = 1.0 if i % 2 else -1.0
    return t


def group_masks():
    m = np.zeros((P, 2, GROUPS), np.float32)
    for ct in range(2):
        for p in range(P):
            c = (0 if p < 64 else 128) + 64 * ct + p % 64
            m[p, ct, c // GC] = 1.0
    return m


def wavelet_preact_kernel(nc, x, h, taps, gmask, out):
    x_rows = x.rearrange("b h w c -> (b h) (w c)")
    out_rows = out.rearrange("b h w c -> (b h) (w c)")
    x_strip = x.rearrange("b h (v t i) c -> i (b h v) t c", v=2, i=WP)
    x_strip_t = x.rearrange("b h (v t i) c -> t (b h v) i c", v=2, i=WP)
    x_stats = x.rearrange("b h w c -> (b h w c)").rearrange("(n p f) -> n p f", p=P, f=POS * C)

    with ExitStack() as ctx:
        def sb(name, shape):
            return ctx.enter_context(nc.sbuf_tensor(name, shape, F32))

        def sem(name):
            return ctx.enter_context(nc.semaphore(name))

        strip = sb("strip", [P, TILES, C])
        resid_ahead = sb("resid_ahead", [P, RING * QS * C])
        stats_in = [sb(f"stats_in{s}", [P, POS * C]) for s in range(2)] + [resid_ahead]
        resid = [sb(f"resid{s}", [P, QS * C]) for s in range(RING)]
        y1 = [[sb(f"y1_{s}{ct}", [P, UW * ROWS]) for ct in range(2)] for s in range(2)]
        records = sb("records", [P, ST_TILES, GROUPS, 6])
        pivot = sb("pivot", [P, GROUPS])
        dev = sb("dev", [P, ST_TILES - 1, GROUPS, 2])
        dev2 = sb("dev2", [P, ST_TILES - 1, GROUPS, 2])
        dev_last = sb("dev_last", [P, 2, GROUPS, 2])
        moments = sb("moments", [P, 2, GROUPS])
        moments_last = sb("moments_last", [P, 2, GROUPS])
        twice = sb("twice", [P, GROUPS])
        shift = sb("shift", [P, GROUPS])
        cross = sb("cross", [P, GROUPS])
        taps_sb = sb("taps_sb", [P, TAPS, NCOEF])
        mask_sb = sb("mask_sb", [P, 2, GROUPS])
        h_sb = sb("h_sb", [P, TAPS])
        coef = [sb(f"coef{s}", [P, NCOEF]) for s in range(2)]
        m_hw = sb("m_hw", [P, 2, N1])
        ones = sb("ones", [P, P])
        part = sb("part", [P, GROUPS])
        gstat = sb("gstat", [P, 2, GROUPS])
        var_sb = sb("var_sb", [P, GROUPS])
        std_sb = sb("std_sb", [P, GROUPS])
        newton = sb("newton", [P, GROUPS])
        picked = sb("picked", [P, 4, GROUPS])
        warm = sb("warm", [P, 1])
        signal = sb("signal", [P, 4])
        chan = sb("chan", [P, 2, 2])
        neg_mr = sb("neg_mr", [P, 2])
        row_sums = sb("row_sums", [P, 2, P])
        mean_lhs = sb("mean_lhs", [P, 2, 2, P])
        m_cr = sb("m_cr", [P, 2, NC2])
        means_w3 = sb("means_w3", [P, 2 * C])

        ps1 = [[ctx.enter_context(nc.psum_tensor(f"ps1_{s}{ct}", [P, 512], F32)) for ct in range(2)] for s in range(2)]
        ps2 = [ctx.enter_context(nc.psum_tensor(f"ps2_{s}", [P, 2, 512], F32)) for s in range(2)]

        consts_loaded = sem("consts_loaded")
        coef_ready = sem("coef_ready")
        dve_chain = sem("dve_chain")
        head_loaded = [sem(f"head_loaded{s}") for s in range(2)]
        last_loaded = [sem(f"last_loaded{s}") for s in range(2)]
        tail_loaded = [sem(f"tail_loaded{s}") for s in range(2)]
        head_used = sem("head_used")
        last_used = sem("last_used")
        stats_loaded = [sem(f"stats_loaded{s}") for s in range(3)]
        stats_used = [sem(f"stats_used{s}") for s in range(3)]
        resid_loaded = [sem(f"resid_loaded{s}") for s in range(RING)]
        stored = [sem(f"stored{s}") for s in range(RING)]
        hw_done = sem("hw_done")
        y1_ready = sem("y1_ready")
        c_done = sem("c_done")
        centred = sem("centred")
        wrapped = sem("wrapped")
        summed = sem("summed")
        part_ready = sem("part_ready")
        part_summed = sem("part_summed")
        var_ready = sem("var_ready")
        std_ready = sem("std_ready")
        mean_lhs_ready = sem("mean_lhs_ready")
        means_done = sem("means_done")
        norm_ready = sem("norm_ready")

        KEPT_LOADED = 16 * (PIECES * FIRST_USES + RING)
        m_c = coef[1][:, O_C:O_C + NC2]
        HEAD = range(0, 2 * TPU)
        TAIL = range(2 * TPU, TILES - 1)
        LAST = TILES - 1

        block = ctx.enter_context(nc.Block())

        @block.sync
        def _(sp):
            sp.dma_start(taps_sb[:, :, :], taps).then_inc(consts_loaded, 16)
            sp.dma_start(mask_sb[:, :, :], gmask).then_inc(consts_loaded, 16)
            sp.dma_start(h_sb[:, :], h.partition_broadcast(P)).then_inc(consts_loaded, 16)

            for free in [hw_done, head_used, last_used] + stats_used:
                sp.sem_inc(free, FREE)

            def load_stats(tile, s, piece, uses):
                if piece == 0:
                    sp.wait_ge(stats_used[s], uses)
                n = POS * C // PIECES
                sp.dma_start(stats_in[s][:, piece * n:(piece + 1) * n],
                             x_stats[bass.ds(tile, 1), :, piece * n:(piece + 1) * n].rearrange("o p f -> (o p) f")
                             ).then_inc(stats_loaded[s], 16)

            def load_ahead(b, quarter):
                for s in range(2 * quarter, 2 * quarter + 2):
                    j, u = divmod(s, UNITS)
                    n = QS * C
                    sp.dma_start(resid_ahead[:, s * n:(s + 1) * n],
                                 x_rows[bass.ds(b * H + j * ROWS, ROWS), u * UW * C:(u + 1) * UW * C]
                                 .rearrange("h (w f) -> w h f", w=16)).then_inc(stats_loaded[2], 16)

            with sp.Fori(0, FIRST_USES) as i:
                for n, s in enumerate(FIRST_ORDER):
                    for piece in range(PIECES):
                        load_stats(i * 3 + (n + 1), s, piece, i + FREE)
            sp.wait_ge(stats_used[2], FIRST_USES + FREE)
            for quarter in range(4):
                load_ahead(0, quarter)

            def load_tiles(row, half, tiles, done):
                for hh in range(2):
                    for wi in range(WP):
                        p0 = hh * 64 + wi * 2 + half
                        sp.dma_start(strip[p0:p0 + 57:8, tiles.start:tiles.stop, :],
                                     x_strip[wi, bass.ds((row + hh * PAIRS) * 2, ROWS), tiles.start:tiles.stop, :]
                                     ).then_inc(done[half], 16)

            def load_last(row, half):
                for hh in range(2):
                    p0 = hh * 64 + half
                    sp.dma_start(strip[p0:p0 + 63:2, LAST, :],
                                 x_strip_t[LAST, bass.ds((row + hh * PAIRS) * 2, ROWS), :, :]
                                 ).then_inc(last_loaded[half], 16)

            def four_chunks(b, i, start=False, end=False):
                before = b * H + (PAIRS - CP)
                for c in range(4):
                    pair, j = divmod(c, 2)
                    row = b * H + i * (4 * CP) + c * CP

                    def load_resid(u):
                        if start and pair == 0:
                            return
                        s = j * UNITS + u
                        sp.wait_ge(stored[s], b * (8 * CHUNKS) + i * 32 + pair * 16)
                        src = x_rows[bass.ds(b * H + i * (4 * ROWS) + c * ROWS, ROWS), u * UW * C:(u + 1) * UW * C]
                        sp.dma_start(resid[s][:, :], src.rearrange("h (w f) -> w h f", w=16)
                                     ).then_inc(resid_loaded[s], 16)

                    def load_piece(half):
                        first = isinstance(b, int) and b == 0 and start
                        last = isinstance(b, int) and b == B - 1
                        following = not (isinstance(b, int) and b == B - 2)
                        if last:
                            return
                        if first and c == 0 and half == 0:
                            for piece in range(2):
                                load_stats(ST_TILES + 1, 0, piece, FIRST_USES + FREE)
                        if end and c in (1, 2):
                            if c == 1 and half == 0:
                                sp.wait_ge(centred, b * UPB + RING)
                            load_ahead(b + 1, 2 * (c - 1) + half)
                        elif j == 0:
                            load_stats(b * ST_TILES + i * 2 + (ST_TILES + pair + 1), pair, 2 + half, None)
                        elif not end or following:
                            uses = b * USES[1 - pair] + i + (FIRST_USES + pair + FREE)
                            load_stats(b * ST_TILES + i * 2 + (ST_TILES + pair + 2), 1 - pair, half, uses)

                    for u in range(2):
                        load_resid(u)
                    sp.wait_ge(head_used, b * CHUNKS + i * 4 + (c + FREE))
                    if start and c == 0:
                        load_tiles(before, 1, HEAD, head_loaded)
                    load_tiles(row, j, HEAD, head_loaded)
                    if not (start and c == 0):
                        load_piece(0)
                    load_resid(2)
                    sp.wait_ge(last_used, b * CHUNKS + i * 4 + (c + FREE))
                    if start and c == 0:
                        load_last(before, 1)
                    load_last(row, j)
                    if start and c == 0:
                        load_piece(0)
                    load_resid(3)
                    sp.wait_ge(hw_done, b * (2 * UPB) + i * (8 * UNITS) + (c * 2 * UNITS + FREE))
                    if start and c == 0:
                        load_tiles(before, 1, TAIL, tail_loaded)
                    load_tiles(row, j, TAIL, tail_loaded)
                    load_piece(1)

            def batch(b):
                four_chunks(b, 0, start=True)
                with sp.Fori(1, CHUNKS // 4 - 1) as i:
                    four_chunks(b, i)
                four_chunks(b, CHUNKS // 4 - 1, end=True)

            batch(0)
            with sp.Fori(1, B - 2) as b:
                batch(b)
            batch(B - 2)
            batch(B - 1)

        @block.gpsimd
        def _(pool):
            def centre(s, b, kk):
                out = resid[s][:, :]
                if isinstance(kk, int) and kk == 0:
                    pool.wait_ge(stats_loaded[2], b * (16 * RING) + KEPT_LOADED)
                    if not (isinstance(b, int) and b == 0):
                        pool.wait_ge(stored[s], b * (8 * CHUNKS))
                    src = resid_ahead[:, s * QS * C:(s + 1) * QS * C]
                else:
                    pool.wait_ge(resid_loaded[s], b * (8 * (CHUNKS - 2)) + kk * 16)
                    src = out
                o3, i3 = (v.rearrange("p (n f) -> p n f", n=2) for v in (out, src))
                m3 = means_w3[:, :].rearrange("p (n f) -> p n f", n=1).broadcast_to([P, 2, 2 * C])
                nc.gpsimd.tensor_tensor(o3, i3, m3, ALU.add).then_inc(centred, 1)

            def store(s, b, kk):
                j, u = divmod(s, UNITS)
                pool.wait_ge(summed, b * (2 * UPB) + kk * (2 * RING) + (2 * s + 2 + SLOTS))
                dst = out_rows[bass.ds(b * H + kk * (2 * ROWS) + j * ROWS, ROWS), u * UW * C:(u + 1) * UW * C]
                pool.dma_start(dst.rearrange("h (w f) -> w h f", w=16), resid[s][:, :]).then_inc(stored[s], 16)

            def pair_steps(b, kk):
                for s in range(RING):
                    if s < UNITS:
                        centre(s + UNITS, b, kk)
                    elif not (isinstance(kk, int) and kk == CHUNKS // 2 - 1):
                        centre(s - UNITS, b, kk + 1)
                    store(s, b, kk)

            def batch(b):
                pool.wait_ge(norm_ready, b + 1)
                for s in range(UNITS):
                    centre(s, b, 0)
                pair_steps(b, 0)
                with pool.Fori(1, CHUNKS // 2 - 1) as kk:
                    pair_steps(b, kk)
                pair_steps(b, CHUNKS // 2 - 1)

            batch(0)
            with pool.Fori(1, B) as b:
                batch(b)
            for s in range(RING):
                pool.wait_ge(stored[s], 16 * B * CHUNKS // 2)

        @block.tensor
        def _(pe):
            pe.wait_ge(coef_ready, 1)

            def rows_width(j, b, kk):
                phase, u = divmod(j, UNITS)
                first = u * TPU
                full = [(t, 0, N1, (t - first) * 2 * WP * ROWS) for t in range(first, first + TPU - 1)]
                edge = (first + TPU - 1, 0, 2 * WP * ROWS, (TPU - 1) * 2 * WP * ROWS)
                halo = ((first - 1) % TILES, 2 * WP * ROWS, N1, 0)

                def product(ct, what, start, stop):
                    t, a, z, at = what
                    return nc.tensor.matmul(ps1[j % 2][ct][:, at:at + z - a], strip[:, t, ct * P:(ct + 1) * P],
                                            m_hw[:, phase, a:z], start=start, stop=stop, skip_group_check=True)

                even = b * (CHUNKS // 2) + kk + 1
                odd = b * (CHUNKS // 2 + 1) + kk + (1 if phase == 0 else 2)

                def strips_in(loaded, per_strip):
                    if phase == 0:
                        pe.wait_ge(loaded[0], even * per_strip)
                    pe.wait_ge(loaded[1], odd * per_strip)

                if u == 0:
                    strips_in(head_loaded, 16 * 2 * WP)
                elif u == 2:
                    strips_in(tail_loaded, 16 * 2 * WP)
                if u == 0:
                    for ct in range(2):
                        for n, what in enumerate(full + [edge]):
                            product(ct, what, n == 0, False)
                    strips_in(last_loaded, 32)
                    for ct in range(2):
                        product(ct, halo, False, True).then_inc(hw_done, 1)
                    return
                lead, rest = (halo, full + [edge]) if u < 3 else (edge, [halo] + full)
                for ct in range(2):
                    mm = product(ct, lead, True, False)
                if u == 2:
                    mm.then_inc(head_used, 1)
                if u == 3:
                    mm.then_inc(last_used, 1)
                for ct in range(2):
                    for n, what in enumerate(rest):
                        mm = product(ct, what, False, n == len(rest) - 1)
                    mm.then_inc(hw_done, 1)

            def channel_product(o, data, m):
                nc.tensor.matmul(o[:, 0:NC2], data[0], m[0], start=True, stop=False, skip_group_check=True)
                return nc.tensor.matmul(o[:, P:P + NC2], data[1], m[1], start=False, stop=True, skip_group_check=True)

            def channels(j, b, kk):
                if j == 0:
                    pe.wait_ge(norm_ready, b + 1)
                pe.wait_ge(y1_ready, b * (2 * UPB) + kk * (2 * RING) + (2 * j + 2))
                for half in range(SLOTS):
                    pe.wait_ge(summed, b * (2 * UPB) + kk * (2 * RING) + (2 * j + half + 1))
                    for n in range(2):
                        q = 2 * half + n
                        mm = channel_product(ps2[half][:, n, :],
                                             [y1[j % 2][ct][:, q * P:(q + 1) * P] for ct in range(2)],
                                             [m_cr[:, ct, :] for ct in range(2)])
                    mm.then_inc(c_done, 1)

            def pair_steps(b, kk, skip=0):
                for j in range(RING):
                    if skip <= j < RING - 1:
                        rows_width(j + 1, b, kk)
                    elif j == RING - 1 and not (isinstance(kk, int) and kk == CHUNKS // 2 - 1):
                        rows_width(0, b, kk + 1)
                    channels(j, b, kk)

            with pe.Fori(0, B) as b:
                rows_width(0, b, 0)
                pe.wait_ge(summed, b * (2 * UPB) + SLOTS)
                for n in range(2):
                    pe.wait_ge(part_ready, b * 2 + (n + 1))
                    nc.tensor.matmul(ps2[0][:, 0, n * GROUPS:(n + 1) * GROUPS], ones[:, :], part[:, :], start=True, stop=True
                                     ).then_inc(part_summed, 1)
                rows_width(1, b, 0)
                pe.wait_ge(mean_lhs_ready, b + 1)
                for a in range(2):
                    mm = channel_product(ps2[1][:, a, :], [mean_lhs[:, ct, a, :] for ct in range(2)], [m_c, m_c])
                mm.then_inc(means_done, 1)
                pair_steps(b, 0, skip=1)
                with pe.Fori(1, CHUNKS // 2 - 1) as kk:
                    pair_steps(b, kk)
                pair_steps(b, CHUNKS // 2 - 1)

        @block.scalar
        def _(act):
            act.wait_ge(coef_ready, 1)
            with act.Fori(0, B) as b:
                nc.scalar.activation(warm[:, :], ones[:, 0:1], ACT.Sqrt)
                act.wait_ge(var_ready, b + 1)
                nc.scalar.activation(std_sb[:, :], var_sb[:, :], ACT.Sqrt).then_inc(std_ready, 1)
                with act.Fori(0, CHUNKS // 2) as kk:
                    for j in range(RING):
                        for ct in range(2):
                            act.wait_ge(hw_done, b * (2 * UPB) + kk * (2 * RING) + (2 * j + ct + 1 + FREE))
                            for z in range(2):
                                src = ps1[j % 2][ct][64 * z:64 * z + 64, :]
                                dst = y1[j % 2][z][64 * ct:64 * ct + 64, :]
                                last = nc.scalar.activation(dst.rearrange("p (q w h) -> p q w h", q=QS, h=ROWS),
                                                            src.rearrange("p (w q h) -> p q w h", q=QS, h=ROWS),
                                                            ACT.Copy)
                            last.then_inc(y1_ready, 1)

        @block.vector
        def _(dve):
            count = [0]

            def link(ins):
                count[0] += 1
                ins.then_inc(dve_chain, 1)
                dve.wait_ge(dve_chain, count[0])

            dve.wait_ge(consts_loaded, 48)
            link(nc.vector.memset(ones[:, :], 1.0 / (2 * ST_TILES * P)))
            link(nc.vector.tensor_scalar(coef[0][:, :], taps_sb[:, 0, :], h_sb[:, 0:1], None, ALU.mult))
            for i in range(1, TAPS):
                link(nc.vector.scalar_tensor_tensor(out=coef[i % 2][:, :], in0=taps_sb[:, i, :], scalar=h_sb[:, i:i + 1],
                                                    in1=coef[(i + 1) % 2][:, :], op0=ALU.mult, op1=ALU.add))
            NW = 2 * WP + HALO
            for phase in range(2):
                a_w = coef[1][:, O_W:O_W + NW].rearrange("p (w o) -> p w o", o=1).broadcast_to([P, NW, ROWS])
                a_h = coef[1][:, O_H + phase * ROWS:O_H + (phase + 1) * ROWS].rearrange("p (o h) -> p o h", o=1
                                                                                        ).broadcast_to([P, NW, ROWS])
                link(nc.vector.tensor_tensor(m_hw[:, phase, :].rearrange("p (w h) -> p w h", h=ROWS), a_w, a_h, ALU.mult))
            for a in range(2):
                for e in range(2):
                    link(nc.vector.tensor_scalar(row_sums[:, a, e:P:2], ones[:, 0:P // 2], float(2 * ST_TILES * P),
                                                 coef[1][:, O_S + e:O_S + e + 1], ALU.mult, ALU.mult))
                link(nc.vector.tensor_scalar(row_sums[:, a, :], row_sums[:, a, :], coef[1][:, O_S + a:O_S + a + 1],
                                             None, ALU.mult))
            SETUP = count[0]
            nc.vector.memset(signal[:, 0:1], 0.0).then_inc(coef_ready, 1)
            nc.vector.memset(signal[:, 1:2], 0.0).then_inc(summed, SLOTS)

            def group_stats(s, k, g0, g1, loads, last):
                if g0 == 0:
                    dve.wait_ge(stats_loaded[s], loads)
                view = stats_in[s][:, :].rearrange("p (s c) -> p s c", c=C)
                for g in range(g0, g1):
                    ins = nc.vector.bn_stats(records[:, bass.ds(k, 1), g, :].rearrange("p o f -> p (o f)"),
                                             view[:, :, g * GC:(g + 1) * GC])
                if last:
                    ins.then_inc(stats_used[s], 1)

            GATHER, FINISH = 5, 18
            RECORDS = 2 * ST_TILES
            PER_RECORD = float(POS * GC // 2)
            flat = "p k g s -> p (k g s)"

            def gather_stats(b, step):
                n = b * (GATHER + FINISH) + (SETUP + step)
                rec = records[:, 0:ST_TILES - 1, :, :].rearrange("p k g (s r) -> p r k g s", r=3)
                if step == 0:
                    for s in range(2):
                        dve.wait_ge(stats_used[s], b * USES[s] + (FIRST_USES + FREE))
                    ins = nc.vector.tensor_copy(pivot[:, :], records[:, 0, :, 1])
                elif step == 1:
                    piv = pivot[:, :].rearrange("p (o g e) -> p o g e", o=1, e=1).broadcast_to([P, ST_TILES - 1, GROUPS, 2])
                    ins = nc.vector.tensor_tensor(dev[:, :, :, :], rec[:, 1], piv, ALU.subtract)
                elif step == 2:
                    d = dev[:, :, :, :].rearrange(flat)
                    ins = nc.vector.scalar_tensor_tensor(out=dev2[:, :, :, :].rearrange(flat), in0=d, scalar=PER_RECORD,
                                                         in1=d, op0=ALU.mult, op1=ALU.mult)
                elif step == 3:
                    nc.vector.tensor_reduce(moments[:, 0, :], dev[:, :, :, :].rearrange("p k g s -> p g k s"),
                                            AX.XY, ALU.add)
                    ins = nc.vector.tensor_tensor(dev2[:, :, :, :], dev2[:, :, :, :], rec[:, 2], ALU.add)
                elif step == 4:
                    ins = nc.vector.tensor_reduce(moments[:, 1, :], dev2[:, :, :, :].rearrange("p k g s -> p g k s"),
                                                  AX.XY, ALU.add)
                ins.then_inc(dve_chain, 1)
                dve.wait_ge(dve_chain, n + 1)

            def finish_stats(b):
                n = [0]

                def link(ins):
                    n[0] += 1
                    ins.then_inc(dve_chain, 1)
                    dve.wait_ge(dve_chain, b * (GATHER + FINISH) + (SETUP + GATHER + n[0]))

                dve.wait_ge(stats_used[2], b + (FIRST_USES + 1 + FREE))
                rec = records[:, ST_TILES - 1, :, :].rearrange("p g (s r) -> p r g s", r=3)
                piv = pivot[:, :].rearrange("p (g e) -> p g e", e=1).broadcast_to([P, GROUPS, 2])
                d, q = (dev_last[:, v].rearrange("p g s -> p (g s)") for v in range(2))
                link(nc.vector.tensor_tensor(dev_last[:, 0], rec[:, 1], piv, ALU.subtract))
                link(nc.vector.scalar_tensor_tensor(out=q, in0=d, scalar=PER_RECORD, in1=d, op0=ALU.mult, op1=ALU.mult))
                link(nc.vector.tensor_tensor(dev_last[:, 1], dev_last[:, 1], rec[:, 2], ALU.add))
                link(nc.vector.tensor_reduce(moments_last[:, :, :], dev_last[:, :, :, :], AX.X, ALU.add))
                link(nc.vector.tensor_tensor(moments[:, :, :], moments[:, :, :], moments_last[:, :, :], ALU.add))
                nc.vector.scalar_tensor_tensor(out=part[:, :], in0=pivot[:, :], scalar=float(RECORDS), in1=moments[:, 0, :],
                                               op0=ALU.mult, op1=ALU.add).then_inc(part_ready, 1)
                link(nc.vector.tensor_scalar(twice[:, :], moments[:, 0, :], -2.0, None, ALU.mult))
                dve.wait_ge(part_summed, b * 2 + 1)
                nc.vector.tensor_copy(gstat[:, 0, :], ps2[0][:, 0, 0:GROUPS])
                link(nc.vector.tensor_tensor(shift[:, :], ps2[0][:, 0, 0:GROUPS], pivot[:, :], ALU.subtract))
                link(nc.vector.scalar_tensor_tensor(out=cross[:, :], in0=shift[:, :], scalar=float(RECORDS),
                                                    in1=twice[:, :], op0=ALU.mult, op1=ALU.add))
                link(nc.vector.tensor_tensor(cross[:, :], cross[:, :], shift[:, :], ALU.mult))
                nc.vector.scalar_tensor_tensor(out=part[:, :], in0=cross[:, :], scalar=PER_RECORD, in1=moments[:, 1, :],
                                               op0=ALU.mult, op1=ALU.add).then_inc(part_ready, 1)
                dve.wait_ge(part_summed, b * 2 + 2)
                nc.vector.tensor_scalar(var_sb[:, :], ps2[0][:, 0, GROUPS:2 * GROUPS], 1.0 / PER_RECORD, EPS,
                                        ALU.mult, ALU.add).then_inc(var_ready, 1)
                dve.wait_ge(std_ready, b + 1)
                r0, vr, r = std_sb[:, :], newton[:, :], gstat[:, 1, :]
                link(nc.vector.reciprocal(r0, std_sb[:, :]))
                link(nc.vector.tensor_tensor(vr, var_sb[:, :], r0, ALU.mult))
                link(nc.vector.tensor_tensor(vr, vr, r0, ALU.mult))
                link(nc.vector.tensor_scalar(vr, vr, -0.5, 1.5, ALU.mult, ALU.add))
                link(nc.vector.tensor_tensor(r, r0, vr, ALU.mult))
                for ct in range(2):
                    for v in range(2):
                        ins = nc.vector.tensor_tensor_reduce(picked[:, 2 * ct + v, :], gstat[:, v, :], mask_sb[:, ct, :],
                                                             1.0, 0.0, ALU.mult, ALU.add, chan[:, v, ct:ct + 1])
                link(ins)
                link(nc.vector.scalar_tensor_tensor(out=neg_mr[:, :], in0=chan[:, 0, :], scalar=-1.0, in1=chan[:, 1, :],
                                                    op0=ALU.mult, op1=ALU.mult))
                for ct in range(2):
                    for a in range(2):
                        ins = nc.vector.tensor_scalar(mean_lhs[:, ct, a, :], row_sums[:, a, :], neg_mr[:, ct:ct + 1],
                                                      None, ALU.mult)
                ins.then_inc(mean_lhs_ready, 1)
                for ct in range(2):
                    ins = nc.vector.tensor_scalar(m_cr[:, ct, :], m_c, chan[:, 1, ct:ct + 1], None, ALU.mult)
                link(ins)
                dve.wait_ge(means_done, b + 1)
                w3 = means_w3[:, :].rearrange("p (a c) -> p a c", c=C)
                link(nc.vector.tensor_copy(w3, ps2[1][:, :, 0:C]))
                nc.vector.tensor_tensor(w3[:, :, 0:HALO], ps2[1][:, :, C:C + HALO], w3[:, :, 0:HALO], ALU.add
                                        ).then_inc(norm_ready, 1)
                assert n[0] == FINISH, n

            with dve.Fori(0, FIRST_USES) as i:
                for n, s in enumerate(FIRST_ORDER):
                    group_stats(s, i * 3 + n, 0, GROUPS, i * (16 * PIECES) + 16 * PIECES, True)
            for step in range(GATHER):
                gather_stats(0, step)
            group_stats(2, ST_TILES - 1, 0, GROUPS, KEPT_LOADED, True)

            def two_pairs(b, i, end=False):
                for unit in range(2 * RING):
                    pair, s = divmod(unit, RING)
                    dve.wait_ge(centred, b * UPB + i * (2 * RING) + (unit + 1))
                    for half in range(SLOTS):
                        r = resid[s][:, half * 2 * C:(half + 1) * 2 * C].rearrange("p (q c) -> p q c", c=C)
                        halves = b * (2 * UPB) + i * (4 * RING) + (2 * unit + half + 1)
                        dve.wait_ge(c_done, halves)
                        nc.vector.tensor_tensor(r[:, :, 0:HALO], ps2[half][:, :, C:C + HALO], r[:, :, 0:HALO], ALU.add
                                                ).then_inc(wrapped, 1)
                        dve.wait_ge(wrapped, halves)
                        nc.vector.tensor_tensor(r, ps2[half][:, :, 0:C], r, ALU.add).then_inc(summed, 1)
                    if isinstance(b, int) and b == B - 1:
                        continue
                    if end and pair == 1 and s < GATHER:
                        gather_stats(b + 1, s)
                    if SHARE[s]:
                        g0 = sum(SHARE[:s])
                        if end and pair == 1:
                            group_stats(2, ST_TILES - 1, g0, g0 + SHARE[s],
                                        (b + 1) * (16 * RING) + KEPT_LOADED, s == RING - 1)
                        else:
                            group_stats(pair, i * 2 + pair, g0, g0 + SHARE[s],
                                        b * (16 * PIECES * USES[pair]) + i * (16 * PIECES)
                                        + 16 * PIECES * (FIRST_USES + 1), s == RING - 1)

            def batch(b):
                finish_stats(b)
                with dve.Fori(0, CHUNKS // 4 - 1) as i:
                    two_pairs(b, i)
                two_pairs(b, CHUNKS // 4 - 1, end=True)

            with dve.Fori(0, B - 1) as b:
                batch(b)
            batch(B - 1)


def kernel(**inputs):
    import numpy as _np
    import concourse.bacc as _bacc
    from concourse import mybir as _mybir
    from concourse.bass_utils import run_bass_kernel_spmd as _run

    nc = _bacc.Bacc("TRN2", target_bir_lowering=False, num_devices=1)
    arrays, args = {}, []
    host = {"x": inputs["x"], "L0_conv_h": inputs["L0_conv_h"], "taps": tap_table(), "gmask": group_masks()}
    for name, a in host.items():
        a = _np.ascontiguousarray(a)
        arrays[f"in_{name}_dram"] = a
        args.append(nc.dram_tensor(f"in_{name}_dram", a.shape, _mybir.dt.from_np(a.dtype), kind="ExternalInput").ap())
    args.append(nc.dram_tensor("out_0_dram", (B, H, W, C), _mybir.dt.from_np(_np.dtype("float32")),
                               kind="ExternalOutput").ap())
    wavelet_preact_kernel(nc, *args)
    r = _run(nc, [arrays], core_ids=[0])
    return r.results[0]["out_0_dram"]
```
